# Optimizing a Trainium2 kernel written in Bass

```python
import numpy as np
import jax
import jax.numpy as jnp

def _softmax(x, axis=-1):
    return jax.nn.softmax(x, axis=axis)

def _gelu(x):
    return jax.nn.gelu(x, approximate=True)

def _silu(x):
    return jax.nn.silu(x)

def _sigmoid(x):
    return jax.nn.sigmoid(x)

def _layernorm(x, axis=-1, eps=1e-05):
    m = jnp.mean(x, axis=axis, keepdims=True)
    v = jnp.var(x, axis=axis, keepdims=True)
    return (x - m) / jnp.sqrt(v + eps)

def _scatter_add(tgt, idx, src, axis=0):
    return tgt.at[idx].add(src)

def _segment_sum(src, seg, n):
    return jax.ops.segment_sum(src, seg, n)
kernel_name = 'mk_adj_seq_d1_adj_r2_d5cb7f'

def setup_inputs(seed: int=0):
    np.random.seed(seed)
    _w = jnp.asarray

    def _rec_inputs():
        import jax
        import jax.numpy as jnp
        _gk = jax.random.key(seed)
        x = -0.0005207 + 1.001 * jax.random.normal(jax.random.fold_in(_gk, 1), (8192, 128), jnp.float32)
        _a = jax.random.bernoulli(jax.random.fold_in(_gk, 2), 0.000244141, (8192, 8192))
        _a = jnp.logical_or(_a, jnp.swapaxes(_a, -1, -2))
        _a = jnp.logical_or(_a, jnp.eye(8192, dtype=bool))
        _af = _a.astype(jnp.float32)
        _af = _af * jax.random.uniform(jax.random.fold_in(_gk, 3), (8192, 8192), jnp.float32, 0.05, 1)
        adj = _af
        return (x, adj)
    x, adj = _rec_inputs()

    def _L0_gnn_setup():
        import jax, jax.numpy as jnp
        import numpy as np
        N = 4096
        D = 128
        LN_EPS = 1e-05
        key = jax.random.key(seed)
        k1, k2, k3, k4 = jax.random.split(key, 4)
        inp = jax.random.normal(k1, (N, D), dtype=jnp.float32)
        adj = jax.random.uniform(k2, (N, N), dtype=jnp.float32)
        weight = jax.random.normal(k3, (D, D), dtype=jnp.float32) * (1.0 / np.sqrt(D))
        self_weight = jax.random.normal(k4, (D, D), dtype=jnp.float32) * (1.0 / np.sqrt(D))
        bias = jnp.zeros((D,), dtype=jnp.float32)
        ln_gamma = jnp.ones((D,), dtype=jnp.float32)
        ln_beta = jnp.zeros((D,), dtype=jnp.float32)
        return {'input': inp, 'adj': adj, 'weight': weight, 'self_weight': self_weight, 'bias': bias, 'ln_gamma': ln_gamma, 'ln_beta': ln_beta}
    _L0_gnn_all = _L0_gnn_setup()
    _L0_gnn_in = {k: v for k, v in _L0_gnn_all.items() if k in ('weight', 'self_weight', 'bias', 'ln_gamma', 'ln_beta')}
    del _L0_gnn_all
    return {'x': x, 'adj': adj, 'L0_gnn_weight': _L0_gnn_in['weight'], 'L0_gnn_self_weight': _L0_gnn_in['self_weight'], 'L0_gnn_bias': _L0_gnn_in['bias'], 'L0_gnn_ln_gamma': _L0_gnn_in['ln_gamma'], 'L0_gnn_ln_beta': _L0_gnn_in['ln_beta']}

def reference(x, adj, L0_gnn_weight, L0_gnn_self_weight, L0_gnn_bias, L0_gnn_ln_gamma, L0_gnn_ln_beta):
    import jax
    import jax.numpy as jnp

    def _L0_gnn_ref(input, adj, weight, self_weight, bias, ln_gamma, ln_beta):
        import jax, jax.numpy as jnp
        import numpy as np
        N = 4096
        D = 128
        LN_EPS = 1e-05
        deg = jnp.sum(adj, axis=0) + 1.0
        dinv = deg ** (-0.5)
        adj_ = dinv[:, None] * adj * dinv[None, :]
        support = input @ weight
        out = adj_ @ support + input @ self_weight + bias
        out = jax.nn.relu(out) + input
        mu = jnp.mean(out, axis=-1, keepdims=True)
        var = jnp.mean((out - mu) ** 2, axis=-1, keepdims=True)
        return (out - mu) * jax.lax.rsqrt(var + LN_EPS) * ln_gamma + ln_beta
    x = _L0_gnn_ref(x, adj, L0_gnn_weight, L0_gnn_self_weight, L0_gnn_bias, L0_gnn_ln_gamma, L0_gnn_ln_beta)
    return x

_drawn_inputs = setup_inputs


def setup_inputs(seed=0):
    import zlib

    import numpy as np

    out = dict(_drawn_inputs(seed))
    spreads = {'L0_gnn_bias': (0.0, 0.1), 'L0_gnn_ln_gamma': (1.0, 0.2), 'L0_gnn_ln_beta': (0.0, 0.1)}
    factors = {}
    for name, (base, spread) in spreads.items():
        noise = np.random.default_rng([zlib.crc32(name.encode()), seed]).standard_normal(out[name].shape)
        drawn = base * np.exp(spread * noise) if base else spread * noise
        out[name] = jnp.asarray(drawn.astype(out[name].dtype))
    for name, factor in factors.items():
        out[name] = (out[name] * factor).astype(out[name].dtype)
    return out
```

```python
from contextlib import ExitStack, contextmanager

import concourse.bass as bass
from concourse import mybir

F32 = mybir.dt.float32
BF16 = mybir.dt.bfloat16
ALU = mybir.AluOpType
ACT = mybir.ActivationFunctionType
AX_X = mybir.AxisListType.X

P = 128
SQ = 32
QUARTERS = P // SQ
ROWS = 512
PLANES = 4
COLS = P * PLANES
SPARE = 2
STAGES = 4
KEPT = 4
EPS = 1e-5


@contextmanager
def steps(engine, start, end, step):
    with engine.Fori(0, (end - start) // step) as i:
        yield i * step + start


def moved(ap, by):
    return bass.AP(tensor=ap.tensor, offset=ap.offset + by, ap=ap.ap)


def gcn_kernel(nc, x, adj, weight, self_weight, bias, gamma, beta, out):
    N, D = x.shape
    assert D == P and N % COLS == 0 and ROWS == COLS
    BLOCKS = N // COLS
    H = N // ROWS
    CHUNKS = BLOCKS * H
    SETS = ROWS // SQ
    ADDED = H - KEPT
    LAST = BLOCKS - 1
    FIXED = H - SPARE
    AHEAD = H + SPARE
    assert H % STAGES == 0 and KEPT == STAGES and LAST % 2 == 1 and SPARE == 2 and FIXED > H - STAGES

    adj_view = adj.rearrange("(h s r) (k a c) -> k h a r s c", s=SETS, r=SQ, a=QUARTERS, c=COLS // QUARTERS)
    x_view = x.rearrange("(k p b) d -> k p (b d)", p=P, b=PLANES)
    out_view = out.rearrange("(k p b) d -> k p (b d)", p=P, b=PLANES)

    with ExitStack() as ctx:
        def sb(name, shape, dt=F32):
            return ctx.enter_context(nc.sbuf_tensor(name, shape, dt))

        def sem(name):
            return ctx.enter_context(nc.semaphore(name))

        store = sb("store", [P, PLANES, (H + SPARE) * ROWS])
        staging = sb("staging", [P, STAGES, SETS * P])
        agg = sb("agg", [P, ADDED, ROWS])
        xs = sb("xs", [P, 2, PLANES, D])
        partial = sb("partial", [P, PLANES, H])
        degree = sb("degree", [P, PLANES])
        minus_half = sb("minus_half", [P, PLANES])
        dinv = sb("dinv", [P, BLOCKS, PLANES])
        junk = sb("junk", [P, 2, ROWS], BF16)

        spare = staging[:, :, :].rearrange("p s f -> p (s f)")
        used = [0]

        def carve(n):
            used[0] += n
            assert used[0] <= STAGES * SETS * P
            return spare[:, used[0] - n:used[0]]

        def planes(ap):
            return ap.rearrange("p (b d) -> p b d", b=PLANES)

        w_sb, ws_sb, ident = carve(D), carve(D), carve(P)
        bias_sb, gamma_sb, beta_sb = carve(D), carve(D), carve(D)
        x_row = [planes(carve(COLS)) for _ in range(4)]
        x_t = [planes(carve(COLS)) for _ in range(2)]
        agg_f = [carve(ROWS) for _ in range(4)]
        pre = [planes(carve(COLS)) for _ in range(2)]
        res = [planes(carve(COLS)) for _ in range(2)]
        stats = [carve(6 * PLANES).rearrange("p (b s) -> p b s", b=PLANES) for _ in range(2)]
        mean_var = [carve(2 * PLANES).rearrange("p (b s) -> p b s", b=PLANES) for _ in range(2)]
        var_eps = [carve(PLANES) for _ in range(2)]
        rstd = [carve(PLANES) for _ in range(2)]
        shift = [carve(PLANES) for _ in range(2)]

        bank = [ctx.enter_context(nc.psum_tensor(f"bank{i}", [P, ROWS], F32)) for i in range(8)]
        kept = bank[:KEPT]
        product = bank[KEPT:]
        xt_ps, self_ps, aggw_ps = bank[0], bank[1], bank[2]

        staged = [sem(f"staged{i}") for i in range(STAGES)]
        x_loaded = [sem(f"x_loaded{i}") for i in range(2)]
        transposed = sem("transposed")
        summed = sem("summed")
        degree_ready = sem("degree_ready")
        reduced = sem("reduced")
        dinv_ready = sem("dinv_ready")
        scaled = sem("scaled")
        multiplied = sem("multiplied")
        added = sem("added")
        half_set = sem("half_set")
        const_loaded = sem("const_loaded")
        ident_zero = sem("ident_zero")
        ident_ready = sem("ident_ready")
        xf_loaded = [sem(f"xf_loaded{i}") for i in range(4)]
        agg_done = sem("agg_done")
        xt_done = sem("xt_done")
        xt_copied = sem("xt_copied")
        self_done = sem("self_done")
        aggw_done = sem("aggw_done")
        self_read = sem("self_read")
        pre_done = sem("pre_done")
        relu_done = sem("relu_done")
        stats_done = sem("stats_done")
        mv_done = sem("mv_done")
        var_done = sem("var_done")
        rstd_done = sem("rstd_done")
        shift_done = sem("shift_done")
        normed = sem("normed")
        gained = sem("gained")
        finished = sem("finished")
        stored = [sem(f"stored{i}") for i in range(2)]

        def row_chunk(t):
            return (t + FIXED) % H if isinstance(t, int) else t - SPARE

        def place(h, par):
            return h + SPARE * par if isinstance(h, int) and h >= FIXED else h

        block = ctx.enter_context(nc.Block())

        @block.sync
        def _(sp):
            def load(k, h, u, leaves=None):
                start = h * (ROWS * N) + k * COLS
                if leaves is not None:
                    start = sp.snap(start)
                    sp.lower_val(start * 4)
                    sp.wait_ge(transposed, leaves)
                for a in range(QUARTERS):
                    src = moved(adj_view[0, 0, a], start)
                    dst = staging[SQ * a:SQ * a + SQ, u, :].rearrange("p (s c) -> p s c", s=SETS)
                    sp.dma_start(dst, src).then_inc(staged[u], 16)

            def block_loads(k, first=False):
                for u in range(STAGES):
                    load(k, row_chunk(u), u, leaves=None if first else k * H + (u + 1 - STAGES))
                with steps(sp, STAGES, H, STAGES) as t:
                    for u in range(STAGES):
                        load(k, row_chunk(t + u), u, leaves=k * H + t + (u + 1 - STAGES))

            block_loads(0, first=True)
            with steps(sp, 1, BLOCKS, 1) as k:
                block_loads(k)

            with steps(sp, 0, H, 2) as f:
                for u in range(2):
                    rows = sp.snap((f + u) * (ROWS * D))
                    sp.wait_ge(finished, f + (u + 1))
                    sp.dma_start(moved(out_view[0], rows),
                                 res[u][:, :, :].rearrange("p b d -> p (b d)")).then_inc(stored[u], 16)
            for u in range(2):
                sp.wait_ge(stored[u], 16 * (H // 2))

        @block.gpsimd
        def _(pool):
            def x_block(k, par, first=False):
                if not first:
                    pool.wait_ge(multiplied, (k - 1) * H)
                pool.dma_start(xs[:, par].rearrange("p b d -> p (b d)"),
                               x_view[bass.ds(k, 1)].rearrange("k p c -> (k p) c")).then_inc(x_loaded[par], 16)

            def power(k):
                pool.wait_ge(degree_ready, k + 1)
                nc.gpsimd.tensor_tensor(dinv[:, bass.ds(k, 1), :].rearrange("p k b -> p (k b)"), degree[:, :],
                                        minus_half[:, :], ALU.pow).then_inc(dinv_ready, 1)

            nc.gpsimd.memset(minus_half[:, :], -0.5).then_inc(half_set, 1)
            x_block(0, 0, first=True)
            x_block(1, 1, first=True)
            nc.gpsimd.memset(agg[:, :, :], 0.0).then_inc(added, ADDED)
            pool.wait_ge(half_set, 1)
            power(0)
            power(1)
            with steps(pool, 2, BLOCKS, 2) as k:
                for par in range(2):
                    x_block(k + par, par)
                    power(k + par)

            pool.wait_ge(transposed, CHUNKS)
            for dst, src in ((w_sb, weight[:, :]), (ws_sb, self_weight[:, :]),
                             (bias_sb, bias.partition_broadcast(P)), (gamma_sb, gamma.partition_broadcast(P)),
                             (beta_sb, beta.partition_broadcast(P))):
                pool.dma_start(dst, src).then_inc(const_loaded, 16)
            for f in range(4):
                pool.dma_start(x_row[f].rearrange("p b d -> p (b d)"), x_view[f]).then_inc(xf_loaded[f], 16)
            nc.gpsimd.memset(ident, 0.0).then_inc(ident_zero, 1)
            pool.wait_ge(ident_zero, 1)
            nc.gpsimd.affine_select(out=ident, in_=ident, compare_op=ALU.not_equal, fill=1.0, base=0,
                                    pattern=[[-1, P]], channel_multiplier=1).then_inc(ident_ready, 1)
            pool.wait_ge(const_loaded, 5 * 16)
            beta_b = beta_sb.unsqueeze(1).to_broadcast([P, PLANES, D])

            def finish(f, u, load):
                v = u % 2
                pool.wait_ge(var_done, f + 1)
                nc.gpsimd.tensor_tensor(rstd[v], var_eps[v], minus_half[:, :], ALU.pow).then_inc(rstd_done, 1)
                pool.wait_ge(gained, f + 1)
                nc.gpsimd.tensor_tensor(res[v], res[v], beta_b, ALU.add).then_inc(finished, 1)
                if load:
                    pool.dma_start(x_row[u].rearrange("p b d -> p (b d)"),
                                   x_view[bass.ds(f + 4, 1)].rearrange("k p c -> (k p) c")).then_inc(xf_loaded[u], 16)

            with steps(pool, 0, H - 4, 4) as f:
                for u in range(4):
                    finish(f + u, u, True)
            for u in range(4):
                finish(H - 4 + u, u, False)

        @block.tensor
        def _(pe):
            def chunk(k, h, u, par, first=False, bank_free=None):
                dst = product[u] if bank_free else kept[u]
                if bank_free == "added":
                    pe.wait_ge(added, (k + 1) * ADDED + (h - KEPT - STAGES + 1))
                if bank_free == "collected":
                    pe.wait_ge(agg_done, h - STAGES + 1)
                rows = bass.ds(place(h, par) * ROWS, ROWS)
                for b in range(PLANES):
                    mm = nc.tensor.matmul(dst[:, :], xs[:, par, b, :], store[:, b, rows],
                                          start=(b == 0 and bool(bank_free or first)), stop=(b == PLANES - 1),
                                          skip_group_check=not bank_free)
                mm.then_inc(multiplied, 1)

            def column_block(k, par, first=False):
                pe.wait_ge(scaled, k + 1)
                for u in range(KEPT):
                    chunk(k, u, u, par, first=first)
                with steps(pe, KEPT, H - STAGES, STAGES) as h:
                    for u in range(STAGES):
                        chunk(k, h + u, u, par, bank_free="added")
                for u in range(STAGES):
                    chunk(k, H - STAGES + u, u, par, bank_free="added")

            column_block(0, 0, first=True)
            with steps(pe, 1, LAST, 2) as k:
                column_block(k, 1)
                column_block(k + 1, 0)

            def turn_x(f, u):
                pe.wait_ge(xf_loaded[u], 16 * (f // 4) + 16)
                for b in range(PLANES):
                    mm = nc.tensor.transpose(xt_ps[:, b * P:b * P + P], x_row[u][:, b, :], ident)
                mm.then_inc(xt_done, 1)

            def dense_terms(f, u):
                v = u % 2
                pe.wait_ge(xt_copied, f + 1)
                if not (isinstance(f, int) and f == 0):
                    pe.wait_ge(self_read, f)
                for b in range(PLANES):
                    mm = nc.tensor.matmul(self_ps[:, b * D:b * D + D], x_t[v][:, b, :], ws_sb, start=True, stop=True)
                mm.then_inc(self_done, 1)
                pe.wait_ge(agg_done, f + 1)
                if not (isinstance(f, int) and f == 0):
                    pe.wait_ge(pre_done, f)
                rows = agg_f[u].rearrange("p (m b) -> p b m", b=PLANES)
                for b in range(PLANES):
                    mm = nc.tensor.matmul(aggw_ps[:, b * D:b * D + D], rows[:, b, :], w_sb, start=True, stop=True)
                mm.then_inc(aggw_done, 1)

            pe.wait_ge(scaled, BLOCKS)
            for u in range(KEPT):
                chunk(LAST, u, u, 1)
            pe.wait_ge(const_loaded, 5 * 16)
            pe.wait_ge(ident_ready, 1)
            pe.wait_ge(agg_done, KEPT)
            for u in range(4):
                turn_x(u, u)
                chunk(LAST, KEPT + u, u, 1, bank_free="added")
                dense_terms(u, u)
            with steps(pe, 4, H - KEPT - 4, 4) as f:
                for u in range(4):
                    turn_x(f + u, u)
                    chunk(LAST, f + (KEPT + u), u, 1, bank_free="collected")
                    dense_terms(f + u, u)
            for u in range(4):
                f = H - KEPT - 4 + u
                turn_x(f, u)
                chunk(LAST, f + KEPT, u, 1, bank_free="collected")
                dense_terms(f, u)
            for u in range(4):
                turn_x(H - 4 + u, u)
                dense_terms(H - 4 + u, u)

        @block.scalar
        def _(act):
            def sum_chunk(k, t, par, first=False):
                act.wait_ge(transposed, k * H + t + 1)
                rows = bass.ds(place(row_chunk(t), par) * ROWS, ROWS)
                for b in range(PLANES):
                    if not (first and b < 2):
                        act.wait_ge(summed, (k * H + t) * PLANES + (b - 1))
                    nc.scalar.activation(junk[:, b % 2, :], store[:, b, rows], ACT.Copy,
                                         accum_out=partial[:, b, bass.ds(t, 1)]).then_inc(summed, 1)

            def sum_block(k, par, first=False):
                if not first:
                    act.wait_ge(degree_ready, k)
                for u in range(STAGES):
                    sum_chunk(k, u, par, first=first and u == 0)
                with steps(act, STAGES, H, STAGES) as t:
                    for u in range(STAGES):
                        sum_chunk(k, t + u, par)

            sum_block(0, 0, first=True)
            with steps(act, 1, LAST, 2) as k:
                sum_block(k, 1)
                sum_block(k + 1, 0)
            sum_block(LAST, 1)

            def copy_xt(f, u):
                act.wait_ge(xt_done, f + 1)
                nc.scalar.activation(x_t[u % 2], xt_ps[:, :].rearrange("p (b m) -> p b m", b=PLANES),
                                     ACT.Copy).then_inc(xt_copied, 1)

            def normalise(f, u):
                v = u % 2
                act.wait_ge(shift_done, f + 1)
                if not (isinstance(f, int) and f < 2):
                    act.wait_ge(stored[v], 16 * (f // 2))
                for b in range(PLANES):
                    last = nc.scalar.activation(res[v][:, b, :], pre[v][:, b, :], ACT.Identity,
                                                scale=rstd[v][:, b:b + 1], bias=shift[v][:, b:b + 1])
                last.then_inc(normed, 1)

            copy_xt(0, 0)
            for f in range(2):
                copy_xt(f + 1, f + 1)
                normalise(f, f)
            with steps(act, 2, H - 2, 2) as f:
                for u in range(2):
                    copy_xt(f + (u + 1), u + 1)
                    normalise(f + u, u)
            copy_xt(H - 1, 1)
            normalise(H - 2, 0)
            normalise(H - 1, 1)

        @block.vector
        def _(dve):
            def transpose(k, t, par):
                u = t % STAGES
                dve.wait_ge(staged[u], (k * (H // STAGES) + t // STAGES + 1) * (16 * QUARTERS))
                at = place(row_chunk(t), par) * ROWS
                dst = store[:, :, at:at + ROWS].rearrange("p b (s r) -> p s b r", r=SQ)
                src = staging[:, u, :].rearrange("p (s c b) -> p s b c", s=SETS, b=PLANES)
                nc.vector.transpose(dst, src).then_inc(transposed, 1)

            def scale_block(k, par):
                dve.wait_ge(summed, (k + 1) * (H * PLANES))
                if not (isinstance(k, int) and k == 0):
                    dve.wait_ge(dinv_ready, k)
                nc.vector.tensor_reduce(degree[:, :], partial[:, :, :], AX_X, ALU.add).then_inc(reduced, 1)
                dve.wait_ge(reduced, k + 1)
                nc.vector.tensor_scalar(degree[:, :], degree[:, :], 1.0, None, ALU.add).then_inc(degree_ready, 1)
                dve.wait_ge(x_loaded[par], (k // 2) * 16 + 16)
                dve.wait_ge(dinv_ready, k + 1)
                d = dinv[:, bass.ds(k, 1), :].rearrange("p k b -> p (k b)").unsqueeze(2).to_broadcast([P, PLANES, D])
                nc.vector.tensor_tensor(xs[:, par], xs[:, par], d, ALU.mult).then_inc(scaled, 1)

            def add(k, h, u):
                dve.wait_ge(multiplied, k * H + h + 1)
                dve.wait_ge(added, k * ADDED + (h - KEPT + 1))
                a = agg[:, bass.ds(h - KEPT, 1), :].rearrange("p h r -> p (h r)")
                nc.vector.tensor_tensor(a, a, product[u][:, :], ALU.add).then_inc(added, 1)

            def refill(k, h, par):
                dve.wait_ge(multiplied, k * H + h + 1)
                t = h + AHEAD - H
                if t < H:
                    transpose(k + 1, t, 1 - par)
                else:
                    transpose(k + 2, t - H, par)

            def column_block(k, par, last=False):
                for h in range(H):
                    if h >= KEPT:
                        add(k, h, h % STAGES)
                    if h == FIXED:
                        scale_block(k + 1, 1 - par)
                    if not (last and h >= FIXED):
                        refill(k, h, par)

            for t in range(H):
                transpose(0, t, 0)
            for t in range(SPARE):
                transpose(1, t, 1)
            scale_block(0, 0)
            with steps(dve, 0, LAST - 1, 2) as k:
                column_block(k, 0)
                column_block(k + 1, 1)
            column_block(LAST - 1, 0, last=True)

            bias_b = bias_sb.unsqueeze(1).to_broadcast([P, PLANES, D])
            gamma_b = gamma_sb.unsqueeze(1).to_broadcast([P, PLANES, D])

            def collect(h, u):
                dve.wait_ge(multiplied, LAST * H + h + 1)
                if isinstance(h, int) and h < KEPT:
                    nc.vector.tensor_copy(agg_f[u], kept[u][:, :]).then_inc(agg_done, 1)
                    return
                dve.wait_ge(aggw_done, h - 4 + 1)
                a = agg[:, bass.ds(h - KEPT, 1), :].rearrange("p h r -> p (h r)")
                nc.vector.tensor_tensor(agg_f[u], a, product[u][:, :], ALU.add).then_inc(agg_done, 1)

            def pre_norm(f, u):
                v = u % 2
                if not (isinstance(f, int) and f < 2):
                    dve.wait_ge(normed, f - 1)
                dve.wait_ge(self_done, f + 1)
                nc.vector.tensor_tensor(pre[v], planes(self_ps[:, :]), bias_b, ALU.add).then_inc(self_read, 1)
                dve.wait_ge(self_read, f + 1)
                dve.wait_ge(aggw_done, f + 1)
                for b in range(PLANES):
                    scale = dinv[:, bass.ds(f, 1), b:b + 1].rearrange("p k b -> p (k b)")
                    last = nc.vector.scalar_tensor_tensor(pre[v][:, b, :], aggw_ps[:, b * D:b * D + D], scale,
                                                          pre[v][:, b, :], ALU.mult, ALU.add)
                last.then_inc(pre_done, 1)

            def moments(f, u, more):
                v = u % 2
                dve.wait_ge(pre_done, f + 1)
                nc.vector.scalar_tensor_tensor(pre[v].rearrange("p b d -> p (b d)"),
                                               pre[v].rearrange("p b d -> p (b d)"), 0.0,
                                               x_row[u].rearrange("p b d -> p (b d)"),
                                               ALU.max, ALU.add).then_inc(relu_done, 1)
                dve.wait_ge(relu_done, f + 1)
                for b in range(PLANES):
                    last = nc.vector.bn_stats(stats[v][:, b, :], pre[v][:, b, :])
                last.then_inc(stats_done, 1)
                dve.wait_ge(stats_done, f + 1)
                if more:
                    collect(f + KEPT, u)
                for b in range(PLANES):
                    last = nc.vector.bn_aggr(mean_var[v][:, b, :], stats[v][:, b, :])
                last.then_inc(mv_done, 1)
                dve.wait_ge(mv_done, f + 1)
                nc.vector.tensor_scalar(var_eps[v], mean_var[v][:, :, 1], EPS, None, ALU.add).then_inc(var_done, 1)

            def shift_of(f, u):
                v = u % 2
                dve.wait_ge(rstd_done, f + 1)
                nc.vector.scalar_tensor_tensor(shift[v], mean_var[v][:, :, 0], -1.0, rstd[v],
                                               ALU.mult, ALU.mult).then_inc(shift_done, 1)

            def gain(f, u):
                dve.wait_ge(normed, f + 1)
                nc.vector.tensor_tensor(res[u % 2], res[u % 2], gamma_b, ALU.mult).then_inc(gained, 1)

            def output(f, u, more=True):
                pre_norm(f, u)
                moments(f, u, more)
                if not (isinstance(f, int) and f == 0):
                    gain(f - 1, (u - 1) % 2)
                shift_of(f, u)

            for h in range(KEPT):
                collect(h, h)
            dve.wait_ge(const_loaded, 5 * 16)
            for f in range(4):
                output(f, f)
            with steps(dve, 4, H - KEPT, 4) as f:
                for u in range(4):
                    output(f + u, u)
            for u in range(4):
                output(H - 4 + u, u, more=False)
            gain(H - 1, 1)


_INS = ["x", "adj", "L0_gnn_weight", "L0_gnn_self_weight", "L0_gnn_bias", "L0_gnn_ln_gamma", "L0_gnn_ln_beta"]
_OUTS = [((8192, 128), "float32")]


def kernel(**inputs):
    import numpy as _np
    import concourse.bacc as _bacc
    from concourse import mybir as _mybir
    from concourse.bass_utils import run_bass_kernel_spmd as _run

    nc = _bacc.Bacc("TRN2", target_bir_lowering=False, num_devices=1)
    arrays, args = {}, []
    for name in _INS:
        a = _np.ascontiguousarray(inputs[name])
        arrays[f"in_{name}_dram"] = a
        args.append(nc.dram_tensor(f"in_{name}_dram", a.shape, _mybir.dt.from_np(a.dtype), kind="ExternalInput").ap())
    for i, (shape, dtype) in enumerate(_OUTS):
        dt = _mybir.dt.from_np(_np.dtype(dtype))
        args.append(nc.dram_tensor(f"out_{i}_dram", shape, dt, kind="ExternalOutput").ap())
    gcn_kernel(nc, *args)
    r = _run(nc, [arrays], core_ids=[0])
    return r.results[0]["out_0_dram"]
```

```python
from contextlib import ExitStack, contextmanager

import concourse.bass as bass
from concourse import mybir

F32 = mybir.dt.float32
BF16 = mybir.dt.bfloat16
ALU = mybir.AluOpType
ACT = mybir.ActivationFunctionType
AX_X = mybir.AxisListType.X

P = 128
SQ = 32
QUARTERS = P // SQ
ROWS = 512
PLANES = 4
COLS = P * PLANES
SPARE = 2
STAGES = 4
KEPT = 6
ROTATING = 2
DVE_PLANES = 2
LAG = 2
EPS = 1e-5


@contextmanager
def steps(engine, start, end, step):
    with engine.Fori(0, (end - start) // step) as i:
        yield i * step + start


def moved(ap, by):
    return bass.AP(tensor=ap.tensor, offset=ap.offset + by, ap=ap.ap)


def gcn_kernel(nc, x, adj, weight, self_weight, bias, gamma, beta, out):
    N, D = x.shape
    assert D == P and N % COLS == 0 and ROWS == COLS
    BLOCKS = N // COLS
    H = N // ROWS
    CHUNKS = BLOCKS * H
    SETS = ROWS // SQ
    ADDED = H - KEPT
    LAST = BLOCKS - 1
    FIXED = H - SPARE
    AHEAD = H + SPARE
    ACT_SUMS = H * PLANES - DVE_PLANES
    assert H % STAGES == 0 and LAST % 2 == 1 and SPARE == 2 and FIXED > H - STAGES
    assert (H - KEPT) % ROTATING == 0 and ROTATING == SPARE and LAG == 2 and KEPT == LAG + 4

    adj_view = adj.rearrange("(h s r) (k a c) -> k h a r s c", s=SETS, r=SQ, a=QUARTERS, c=COLS // QUARTERS)
    x_view = x.rearrange("(k p b) d -> k p (b d)", p=P, b=PLANES)
    out_view = out.rearrange("(k p b) d -> k p (b d)", p=P, b=PLANES)

    with ExitStack() as ctx:
        def sb(name, shape, dt=F32):
            return ctx.enter_context(nc.sbuf_tensor(name, shape, dt))

        def sem(name):
            return ctx.enter_context(nc.semaphore(name))

        store = sb("store", [P, PLANES, (H + SPARE) * ROWS])
        staging = sb("staging", [P, STAGES, SETS * P])
        agg = sb("agg", [P, ADDED, ROWS])
        xs = sb("xs", [P, 2, PLANES, D])
        partial = sb("partial", [P, PLANES, H])
        degree = sb("degree", [P, PLANES])
        minus_half = sb("minus_half", [P, PLANES])
        dinv = sb("dinv", [P, BLOCKS, PLANES])
        junk = sb("junk", [P, 2, ROWS], BF16)

        spare = staging[:, :, :].rearrange("p s f -> p (s f)")
        used = [0]

        def carve(n):
            used[0] += n
            assert used[0] <= STAGES * SETS * P
            return spare[:, used[0] - n:used[0]]

        def planes(ap):
            return ap.rearrange("p (b d) -> p b d", b=PLANES)

        w_sb, ws_sb, ident = carve(D), carve(D), carve(P)
        bias_sb, gamma_sb, beta_sb = carve(D), carve(D), carve(D)
        x_row = [planes(carve(COLS)) for _ in range(4)]
        x_t = [planes(carve(COLS)) for _ in range(2)]
        agg_f = [carve(ROWS) for _ in range(4)]
        stats = [carve(6 * PLANES).rearrange("p (b s) -> p b s", b=PLANES) for _ in range(4)]
        mean_var = [carve(2 * PLANES).rearrange("p (b s) -> p b s", b=PLANES) for _ in range(4)]
        var_eps = [carve(PLANES) for _ in range(4)]
        rstd = [carve(PLANES) for _ in range(4)]
        shift = [carve(PLANES) for _ in range(4)]
        pre = [planes(store[:, b, 0:ROWS]) for b in range(4)]
        res = [planes(store[:, b, ROWS:2 * ROWS]) for b in range(4)]

        bank = [ctx.enter_context(nc.psum_tensor(f"bank{i}", [P, ROWS], F32)) for i in range(8)]
        kept = bank[:KEPT]
        product = bank[KEPT:]
        xt_ps = kept[0]

        def self_ps(f):
            return product[0] if isinstance(f, int) and f == 0 else kept[1]

        def aggw_ps(f, u):
            return product[1] if isinstance(f, int) and f == 0 else kept[3 - u % 2]

        staged = [sem(f"staged{i}") for i in range(STAGES)]
        x_loaded = [sem(f"x_loaded{i}") for i in range(2)]
        transposed = sem("transposed")
        summed = sem("summed")
        last_summed = sem("last_summed")
        degree_ready = sem("degree_ready")
        reduced = sem("reduced")
        dinv_ready = sem("dinv_ready")
        scaled = sem("scaled")
        multiplied = sem("multiplied")
        added = sem("added")
        half_set = sem("half_set")
        const_loaded = sem("const_loaded")
        ident_zero = sem("ident_zero")
        ident_ready = sem("ident_ready")
        xf_loaded = [sem(f"xf_loaded{i}") for i in range(4)]
        agg_done = sem("agg_done")
        xt_done = sem("xt_done")
        xt_copied = sem("xt_copied")
        self_done = sem("self_done")
        self_read = sem("self_read")
        biased = sem("biased")
        aggw_done = sem("aggw_done")
        pre_done = sem("pre_done")
        relu_done = sem("relu_done")
        stats_done = sem("stats_done")
        mv_done = sem("mv_done")
        var_done = sem("var_done")
        rstd_done = sem("rstd_done")
        shift_done = sem("shift_done")
        normed = sem("normed")
        gained = sem("gained")
        finished = sem("finished")
        stored = [sem(f"stored{i}") for i in range(4)]

        def row_chunk(t):
            return (t + FIXED) % H if isinstance(t, int) else t - SPARE

        def place(h, par):
            return h + SPARE * par if isinstance(h, int) and h >= FIXED else h

        block = ctx.enter_context(nc.Block())

        @block.sync
        def _(sp):
            def load(k, h, u, leaves=None):
                start = h * (ROWS * N) + k * COLS
                if leaves is not None:
                    start = sp.snap(start)
                    sp.lower_val(start * 4)
                    sp.wait_ge(transposed, leaves)
                for a in range(QUARTERS):
                    src = moved(adj_view[0, 0, a], start)
                    dst = staging[SQ * a:SQ * a + SQ, u, :].rearrange("p (s c) -> p s c", s=SETS)
                    sp.dma_start(dst, src).then_inc(staged[u], 16)

            def block_loads(k, first=False):
                for u in range(STAGES):
                    load(k, row_chunk(u), u, leaves=None if first else k * H + (u + 1 - STAGES))
                with steps(sp, STAGES, H, STAGES) as t:
                    for u in range(STAGES):
                        load(k, row_chunk(t + u), u, leaves=k * H + t + (u + 1 - STAGES))

            block_loads(0, first=True)
            with steps(sp, 1, BLOCKS, 1) as k:
                block_loads(k)

            with steps(sp, 0, H, 4) as f:
                for u in range(4):
                    rows = sp.snap((f + u) * (ROWS * D))
                    sp.lower_val(rows * 4)
                    sp.wait_ge(finished, f + (u + 1))
                    sp.dma_start(moved(out_view[0], rows), res[u].rearrange("p b d -> p (b d)")).then_inc(stored[u], 16)
            for u in range(4):
                sp.wait_ge(stored[u], 16 * (H // 4))

        @block.gpsimd
        def _(pool):
            def x_block(k, par, first=False):
                if not first:
                    pool.wait_ge(multiplied, (k - 1) * H)
                pool.dma_start(xs[:, par].rearrange("p b d -> p (b d)"),
                               x_view[bass.ds(k, 1)].rearrange("k p c -> (k p) c")).then_inc(x_loaded[par], 16)

            def power(k):
                pool.wait_ge(degree_ready, k + 1)
                nc.gpsimd.tensor_tensor(dinv[:, bass.ds(k, 1), :].rearrange("p k b -> p (k b)"), degree[:, :],
                                        minus_half[:, :], ALU.pow).then_inc(dinv_ready, 1)

            nc.gpsimd.memset(minus_half[:, :], -0.5).then_inc(half_set, 1)
            x_block(0, 0, first=True)
            x_block(1, 1, first=True)
            nc.gpsimd.memset(agg[:, :, :], 0.0).then_inc(added, ADDED)
            pool.wait_ge(half_set, 1)
            power(0)
            power(1)
            with steps(pool, 2, BLOCKS, 2) as k:
                for par in range(2):
                    x_block(k + par, par)
                    power(k + par)

            pool.wait_ge(transposed, CHUNKS)
            for dst, src in ((w_sb, weight[:, :]), (ws_sb, self_weight[:, :]),
                             (bias_sb, bias.partition_broadcast(P)), (gamma_sb, gamma.partition_broadcast(P)),
                             (beta_sb, beta.partition_broadcast(P))):
                pool.dma_start(dst, src).then_inc(const_loaded, 16)
            for f in range(4):
                pool.dma_start(x_row[f].rearrange("p b d -> p (b d)"), x_view[f]).then_inc(xf_loaded[f], 16)
            nc.gpsimd.memset(ident, 0.0).then_inc(ident_zero, 1)
            pool.wait_ge(ident_zero, 1)
            nc.gpsimd.affine_select(out=ident, in_=ident, compare_op=ALU.not_equal, fill=1.0, base=0,
                                    pattern=[[-1, P]], channel_multiplier=1).then_inc(ident_ready, 1)
            pool.wait_ge(const_loaded, 5 * 16)
            bias_b = bias_sb.unsqueeze(1).to_broadcast([P, PLANES, D])
            beta_b = beta_sb.unsqueeze(1).to_broadcast([P, PLANES, D])

            def add_beta(f, u):
                pool.wait_ge(gained, f + 1)
                nc.gpsimd.tensor_tensor(res[u], res[u], beta_b, ALU.add).then_inc(finished, 1)

            def add_bias(f, u):
                pool.wait_ge(self_read, f + 1)
                nc.gpsimd.tensor_tensor(pre[u], pre[u], bias_b, ALU.add).then_inc(biased, 1)

            def output(f, u, reload=False):
                if not isinstance(f, int) or f + 1 < H:
                    add_bias(f + 1, (u + 1) % 4)
                if reload:
                    pool.wait_ge(relu_done, f + 1)
                    pool.dma_start(x_row[u].rearrange("p b d -> p (b d)"),
                                   x_view[bass.ds(f + 4, 1)].rearrange("k p c -> (k p) c")).then_inc(xf_loaded[u], 16)
                pool.wait_ge(var_done, f + 1)
                nc.gpsimd.tensor_tensor(rstd[u], var_eps[u], minus_half[:, :], ALU.pow).then_inc(rstd_done, 1)
                if not (isinstance(f, int) and f < 2):
                    add_beta(f - 2, (u - 2) % 4)

            add_bias(0, 0)
            for u in range(4):
                output(u, u, reload=True)
            with steps(pool, 4, H - 4, 4) as f:
                for u in range(4):
                    output(f + u, u, reload=True)
            for u in range(4):
                output(H - 4 + u, u)
            add_beta(H - 2, 2)
            add_beta(H - 1, 3)

        @block.tensor
        def _(pe):
            def chunk(k, h, u, par, first=False):
                in_kept = isinstance(h, int) and h < KEPT
                dst = kept[u] if in_kept else product[u]
                rows = bass.ds(place(h, par) * ROWS, ROWS)
                for b in range(PLANES):
                    mm = nc.tensor.matmul(dst[:, :], xs[:, par, b, :], store[:, b, rows],
                                          start=b == 0 and (first or not in_kept), stop=b == PLANES - 1,
                                          skip_group_check=in_kept)
                mm.then_inc(multiplied, 1)

            def column_block(k, par, first=False):
                pe.wait_ge(scaled, k + 1)
                for u in range(KEPT):
                    chunk(k, u, u, par, first=first)

                def rotating(h, u):
                    pe.wait_ge(added, (k + 1) * ADDED + (h - KEPT - ROTATING + 1))
                    chunk(k, h, u, par)

                with steps(pe, KEPT, FIXED, ROTATING) as h:
                    for u in range(ROTATING):
                        rotating(h + u, u)
                for u in range(ROTATING):
                    rotating(FIXED + u, u)

            column_block(0, 0, first=True)
            with steps(pe, 1, LAST, 2) as k:
                column_block(k, 1)
                column_block(k + 1, 0)

            def turn_x(f, u):
                pe.wait_ge(xf_loaded[u], 16 * (f // 4) + 16)
                for b in range(PLANES):
                    mm = nc.tensor.transpose(xt_ps[:, b * P:b * P + P], x_row[u][:, b, :], ident)
                mm.then_inc(xt_done, 1)

            def self_term(f, u):
                pe.wait_ge(xt_copied, f + 1)
                if isinstance(f, int) and f == 1:
                    pe.wait_ge(agg_done, 2)
                if not (isinstance(f, int) and f <= 1):
                    pe.wait_ge(self_read, f)
                for b in range(PLANES):
                    mm = nc.tensor.matmul(self_ps(f)[:, b * D:b * D + D], x_t[u % 2][:, b, :], ws_sb,
                                          start=True, stop=True)
                mm.then_inc(self_done, 1)

            def agg_term(f, u):
                if isinstance(f, int) and f < 3:
                    pe.wait_ge(agg_done, [1, 3, 4][f])
                else:
                    pe.wait_ge(agg_done, f + 1)
                    pe.wait_ge(pre_done, f - 1)
                rows = agg_f[u].rearrange("p (m b) -> p b m", b=PLANES)
                for b in range(PLANES):
                    mm = nc.tensor.matmul(aggw_ps(f, u)[:, b * D:b * D + D], rows[:, b, :], w_sb, start=True, stop=True)
                mm.then_inc(aggw_done, 1)

            def output(f, u):
                if not isinstance(f, int) or f + 1 < H:
                    turn_x(f + 1, (u + 1) % 4)
                h = f + LAG
                if not isinstance(h, int) or h < H:
                    if not isinstance(h, int) or h >= KEPT:
                        pe.wait_ge(agg_done, h - ROTATING + 1)
                    chunk(LAST, h, h if isinstance(h, int) and h < KEPT else u % ROTATING, 1)
                if not isinstance(f, int) or f + 1 < H:
                    self_term(f + 1, (u + 1) % 4)
                agg_term(f, u)

            pe.wait_ge(scaled, BLOCKS)
            for u in range(LAG):
                chunk(LAST, u, u, 1)
            pe.wait_ge(const_loaded, 5 * 16)
            pe.wait_ge(ident_ready, 1)
            pe.wait_ge(agg_done, 1)
            turn_x(0, 0)
            pe.wait_ge(added, BLOCKS * ADDED)
            self_term(0, 0)
            for u in range(4):
                output(u, u)
            with steps(pe, 4, H - 4, 4) as f:
                for u in range(4):
                    output(f + u, u)
            for u in range(4):
                output(H - 4 + u, u)

        @block.scalar
        def _(act):
            def sum_chunk(k, t, par, first=False, count=PLANES):
                act.wait_ge(transposed, k * H + t + 1)
                rows = bass.ds(place(row_chunk(t), par) * ROWS, ROWS)
                for b in range(count):
                    if not (first and b < 2):
                        act.wait_ge(summed, k * ACT_SUMS + t * PLANES + (b - 1))
                    nc.scalar.activation(junk[:, b % 2, :], store[:, b, rows], ACT.Copy,
                                         accum_out=partial[:, b, bass.ds(t, 1)]).then_inc(summed, 1)

            def sum_block(k, par, first=False):
                if not first:
                    act.wait_ge(degree_ready, k)
                for u in range(STAGES):
                    sum_chunk(k, u, par, first=first and u == 0)
                with steps(act, STAGES, H - STAGES, STAGES) as t:
                    for u in range(STAGES):
                        sum_chunk(k, t + u, par)
                for t in range(H - STAGES, H):
                    sum_chunk(k, t, par, count=PLANES if t < H - 1 else PLANES - DVE_PLANES)

            sum_block(0, 0, first=True)
            with steps(act, 1, LAST, 2) as k:
                sum_block(k, 1)
                sum_block(k + 1, 0)
            sum_block(LAST, 1)

            def copy_xt(f, u):
                act.wait_ge(xt_done, f + 1)
                nc.scalar.activation(x_t[u % 2], xt_ps[:, :].rearrange("p (b m) -> p b m", b=PLANES),
                                     ACT.Copy).then_inc(xt_copied, 1)

            def copy_self(f, u):
                if not (isinstance(f, int) and f < 4):
                    act.wait_ge(normed, f - 3)
                act.wait_ge(self_done, f + 1)
                nc.scalar.activation(pre[u], planes(self_ps(f)[:, :]), ACT.Copy).then_inc(self_read, 1)

            def normalise(f, u):
                act.wait_ge(shift_done, f + 1)
                if not (isinstance(f, int) and f < 4):
                    act.wait_ge(stored[u], 16 * (f // 4))
                for b in range(PLANES):
                    last = nc.scalar.activation(res[u][:, b, :], pre[u][:, b, :], ACT.Identity,
                                                scale=rstd[u][:, b:b + 1], bias=shift[u][:, b:b + 1])
                last.then_inc(normed, 1)

            def output(f, u):
                if not isinstance(f, int) or f + 1 < H:
                    copy_self(f + 1, (u + 1) % 4)
                if not isinstance(f, int) or f + 2 < H:
                    copy_xt(f + 2, (u + 2) % 4)
                if not (isinstance(f, int) and f == 0):
                    normalise(f - 1, (u - 1) % 4)

            copy_xt(0, 0)
            copy_self(0, 0)
            copy_xt(1, 1)
            for u in range(4):
                output(u, u)
            with steps(act, 4, H - 4, 4) as f:
                for u in range(4):
                    output(f + u, u)
            for u in range(4):
                output(H - 4 + u, u)
            normalise(H - 1, 3)

        @block.vector
        def _(dve):
            def transpose(k, t, par):
                u = t % STAGES
                dve.wait_ge(staged[u], (k * (H // STAGES) + t // STAGES + 1) * (16 * QUARTERS))
                at = place(row_chunk(t), par) * ROWS
                dst = store[:, :, at:at + ROWS].rearrange("p b (s r) -> p s b r", r=SQ)
                src = staging[:, u, :].rearrange("p (s c b) -> p s b c", s=SETS, b=PLANES)
                nc.vector.transpose(dst, src).then_inc(transposed, 1)

            def sum_last(k, par):
                if not (isinstance(k, int) and k == 0):
                    dve.wait_ge(degree_ready, k)
                dve.wait_ge(transposed, (k + 1) * H)
                at = place(row_chunk(H - 1), par) * ROWS
                nc.vector.tensor_reduce(partial[:, PLANES - DVE_PLANES:, H - 1], store[:, PLANES - DVE_PLANES:, at:at + ROWS],
                                        AX_X, ALU.add).then_inc(last_summed, 1)

            def scale_block(k, par):
                dve.wait_ge(summed, (k + 1) * ACT_SUMS)
                dve.wait_ge(last_summed, k + 1)
                if not (isinstance(k, int) and k == 0):
                    dve.wait_ge(dinv_ready, k)
                nc.vector.tensor_reduce(degree[:, :], partial[:, :, :], AX_X, ALU.add).then_inc(reduced, 1)
                dve.wait_ge(reduced, k + 1)
                nc.vector.tensor_scalar(degree[:, :], degree[:, :], 1.0, None, ALU.add).then_inc(degree_ready, 1)
                dve.wait_ge(x_loaded[par], (k // 2) * 16 + 16)
                dve.wait_ge(dinv_ready, k + 1)
                d = dinv[:, bass.ds(k, 1), :].rearrange("p k b -> p (k b)").unsqueeze(2).to_broadcast([P, PLANES, D])
                nc.vector.tensor_tensor(xs[:, par], xs[:, par], d, ALU.mult).then_inc(scaled, 1)

            def add(k, h, u):
                dve.wait_ge(multiplied, k * H + h + 1)
                dve.wait_ge(added, k * ADDED + (h - KEPT + 1))
                a = agg[:, bass.ds(h - KEPT, 1), :].rearrange("p h r -> p (h r)")
                nc.vector.tensor_tensor(a, a, product[u][:, :], ALU.add).then_inc(added, 1)

            def refill(k, h, par):
                dve.wait_ge(multiplied, k * H + h + 1)
                t = h + AHEAD - H
                if t < H:
                    transpose(k + 1, t, 1 - par)
                else:
                    transpose(k + 2, t - H, par)

            def column_block(k, par, last=False):
                for h in range(H):
                    if h >= KEPT:
                        add(k, h, (h - KEPT) % ROTATING)
                    if h == FIXED:
                        scale_block(k + 1, 1 - par)
                    if not (last and h >= FIXED):
                        refill(k, h, par)
                    if h == FIXED - 1:
                        sum_last(k + 1, 1 - par)

            for t in range(H):
                transpose(0, t, 0)
            sum_last(0, 0)
            scale_block(0, 0)
            for t in range(SPARE):
                transpose(1, t, 1)
            with steps(dve, 0, LAST - 1, 2) as k:
                column_block(k, 0)
                column_block(k + 1, 1)
            column_block(LAST - 1, 0, last=True)

            gamma_b = gamma_sb.unsqueeze(1).to_broadcast([P, PLANES, D])

            def collect(h, u):
                if not (isinstance(h, int) and h < 4):
                    dve.wait_ge(aggw_done, h - 3)
                dve.wait_ge(multiplied, LAST * H + h + 1)
                if isinstance(h, int) and h < KEPT:
                    nc.vector.tensor_copy(agg_f[u], kept[h][:, :]).then_inc(agg_done, 1)
                else:
                    a = agg[:, bass.ds(h - KEPT, 1), :].rearrange("p h r -> p (h r)")
                    nc.vector.tensor_tensor(agg_f[u], a, product[u % ROTATING][:, :], ALU.add).then_inc(agg_done, 1)

            def gain(f, u):
                dve.wait_ge(normed, f + 1)
                nc.vector.tensor_tensor(res[u], res[u], gamma_b, ALU.mult).then_inc(gained, 1)

            def shift_of(f, u):
                dve.wait_ge(rstd_done, f + 1)
                nc.vector.scalar_tensor_tensor(shift[u], mean_var[u][:, :, 0], -1.0, rstd[u],
                                               ALU.mult, ALU.mult).then_inc(shift_done, 1)

            def output(f, u):
                h = f + LAG
                if not isinstance(h, int) or h < H:
                    collect(h, (u + LAG) % 4)
                if not (isinstance(f, int) and f < 2):
                    gain(f - 2, (u - 2) % 4)
                dve.wait_ge(biased, f + 1)
                dve.wait_ge(aggw_done, f + 1)
                for b in range(PLANES):
                    scale = dinv[:, bass.ds(f, 1), b:b + 1].rearrange("p k b -> p (k b)")
                    last = nc.vector.scalar_tensor_tensor(pre[u][:, b, :], aggw_ps(f, u)[:, b * D:b * D + D], scale,
                                                          pre[u][:, b, :], ALU.mult, ALU.add)
                last.then_inc(pre_done, 1)
                dve.wait_ge(pre_done, f + 1)
                nc.vector.scalar_tensor_tensor(pre[u].rearrange("p b d -> p (b d)"),
                                               pre[u].rearrange("p b d -> p (b d)"), 0.0,
                                               x_row[u].rearrange("p b d -> p (b d)"),
                                               ALU.max, ALU.add).then_inc(relu_done, 1)
                dve.wait_ge(relu_done, f + 1)
                for b in range(PLANES):
                    last = nc.vector.bn_stats(stats[u][:, b, :], pre[u][:, b, :])
                last.then_inc(stats_done, 1)
                dve.wait_ge(stats_done, f + 1)
                if not (isinstance(f, int) and f == 0):
                    shift_of(f - 1, (u - 1) % 4)
                for b in range(PLANES):
                    last = nc.vector.bn_aggr(mean_var[u][:, b, :], stats[u][:, b, :])
                last.then_inc(mv_done, 1)
                dve.wait_ge(mv_done, f + 1)
                nc.vector.tensor_scalar(var_eps[u], mean_var[u][:, :, 1], EPS, None, ALU.add).then_inc(var_done, 1)

            for h in range(LAG):
                collect(h, h)
            dve.wait_ge(const_loaded, 5 * 16)
            for f in range(4):
                output(f, f)
            with steps(dve, 4, H - 4, 4) as f:
                for u in range(4):
                    output(f + u, u)
            for u in range(4):
                output(H - 4 + u, u)
            gain(H - 2, 2)
            shift_of(H - 1, 3)
            gain(H - 1, 3)


_INS = ["x", "adj", "L0_gnn_weight", "L0_gnn_self_weight", "L0_gnn_bias", "L0_gnn_ln_gamma", "L0_gnn_ln_beta"]
_OUTS = [((8192, 128), "float32")]


def kernel(**inputs):
    import numpy as _np
    import concourse.bacc as _bacc
    from concourse import mybir as _mybir
    from concourse.bass_utils import run_bass_kernel_spmd as _run

    nc = _bacc.Bacc("TRN2", target_bir_lowering=False, num_devices=1)
    arrays, args = {}, []
    for name in _INS:
        a = _np.ascontiguousarray(inputs[name])
        arrays[f"in_{name}_dram"] = a
        args.append(nc.dram_tensor(f"in_{name}_dram", a.shape, _mybir.dt.from_np(a.dtype), kind="ExternalInput").ap())
    for i, (shape, dtype) in enumerate(_OUTS):
        dt = _mybir.dt.from_np(_np.dtype(dtype))
        args.append(nc.dram_tensor(f"out_{i}_dram", shape, dt, kind="ExternalOutput").ap())
    gcn_kernel(nc, *args)
    r = _run(nc, [arrays], core_ids=[0])
    return r.results[0]["out_0_dram"]
```

```python
from contextlib import ExitStack, contextmanager

import concourse.bass as bass
from concourse import mybir

F32 = mybir.dt.float32
BF16 = mybir.dt.bfloat16
ALU = mybir.AluOpType
ACT = mybir.ActivationFunctionType
AX_X = mybir.AxisListType.X

P = 128
SQ = 32
QUARTERS = P // SQ
ROWS = 512
PLANES = 4
COLS = P * PLANES
SPARE = 2
STAGES = 4
KEPT = 6
ROTATING = 2
HALVES = 2
EARLY = 8
EARLY_LEFT = 3
DVE_PLANES = 2
SYNC_QUARTERS = (0, 1)
SCALAR_QUARTERS = (2, 3)
FIRST_QUARTERS = (0, 2, 1, 3)
LAG = 2
EPS = 1e-5


@contextmanager
def steps(engine, start, end, step):
    with engine.Fori(0, (end - start) // step) as i:
        yield i * step + start


def moved(ap, by):
    return bass.AP(tensor=ap.tensor, offset=ap.offset + by, ap=ap.ap)


def gcn_kernel(nc, x, adj, weight, self_weight, bias, gamma, beta, out):
    N, D = x.shape
    assert D == P and N % COLS == 0 and ROWS == COLS
    BLOCKS = N // COLS
    H = N // ROWS
    CHUNKS = BLOCKS * H
    SETS = ROWS // SQ
    ADDED = H - KEPT
    LAST = BLOCKS - 1
    FIXED = H - SPARE
    AHEAD = H + SPARE
    ACT_SUMS = H * PLANES - DVE_PLANES
    HALF = PLANES // HALVES
    HALF_CHUNKS = H // HALVES
    TILES = HALVES * ROWS // P
    GROUPS = HALVES * HALF
    assert HALVES == 2 and HALF_CHUNKS % STAGES == 0 and GROUPS == 4 and LAG <= 2
    assert HALVES * HALF_CHUNKS // STAGES == QUARTERS
    assert H % STAGES == 0 and LAST % 2 == 1 and SPARE == 2 and FIXED > H - STAGES
    assert (H - KEPT) % ROTATING == 0 and ROTATING == SPARE and LAG == 2 and KEPT == LAG + 4

    adj_view = adj.rearrange("(h s r) (k a c) -> k h a r s c", s=SETS, r=SQ, a=QUARTERS, c=COLS // QUARTERS)
    first_view = adj.rearrange("(g m p) (k s c) -> k s g p m c", m=TILES, p=P, s=HALVES, c=COLS // HALVES)
    first_x_view = x.rearrange("(k s p b) d -> k p s (b d)", p=P, s=HALVES, b=HALF)
    first_out_view = out.rearrange("(k s p b) d -> k p s (b d)", p=P, s=HALVES, b=HALF)
    x_squares_view = x.rearrange("(k s r) (a c) -> k a r s c", s=SETS, r=SQ, a=QUARTERS)
    x_view = x.rearrange("(k p b) d -> k p (b d)", p=P, b=PLANES)
    out_view = out.rearrange("(k p b) d -> k p (b d)", p=P, b=PLANES)

    with ExitStack() as ctx:
        def sb(name, shape, dt=F32):
            return ctx.enter_context(nc.sbuf_tensor(name, shape, dt))

        def sem(name):
            return ctx.enter_context(nc.semaphore(name))

        store = sb("store", [P, PLANES, (H + SPARE) * ROWS])
        staging = sb("staging", [P, STAGES, SETS * P])
        agg = sb("agg", [P, ADDED, ROWS])
        xs = sb("xs", [P, 2, PLANES, D])
        partial = sb("partial", [P, PLANES, H])
        degree = sb("degree", [P, PLANES])
        minus_half = sb("minus_half", [P, PLANES])
        dinv = sb("dinv", [P, BLOCKS, PLANES])
        junk = sb("junk", [P, 2, ROWS], BF16)
        w_sb, ws_sb, ident = sb("w_sb", [P, D])[:, :], sb("ws_sb", [P, D])[:, :], sb("ident", [P, P])[:, :]
        bias_sb, gamma_sb, beta_sb = (sb(name, [P, D])[:, :] for name in ("bias_sb", "gamma_sb", "beta_sb"))

        spare = staging[:, :, :].rearrange("p s f -> p (s f)")
        used = [0]

        def carve(n):
            used[0] += n
            assert used[0] <= STAGES * SETS * P
            return spare[:, used[0] - n:used[0]]

        def planes(ap):
            return ap.rearrange("p (b d) -> p b d", b=PLANES)

        x_row = [planes(carve(COLS)) for _ in range(4)]
        x_squares = [carve(ROWS) for _ in range(4)]
        x_t = [carve(ROWS) for _ in range(2)]
        agg_f = [carve(ROWS) for _ in range(4)]
        stats = [carve(6 * PLANES).rearrange("p (b s) -> p b s", b=PLANES) for _ in range(4)]
        mean_var = [carve(2 * PLANES).rearrange("p (b s) -> p b s", b=PLANES) for _ in range(4)]
        var_eps = [carve(PLANES) for _ in range(4)]
        rstd = [carve(PLANES) for _ in range(4)]
        shift = [carve(PLANES) for _ in range(4)]
        pre = [planes(store[:, b, 0:ROWS]) for b in range(4)]
        res = [planes(store[:, b, ROWS:2 * ROWS]) for b in range(4)]

        bank = [ctx.enter_context(nc.psum_tensor(f"bank{i}", [P, ROWS], F32)) for i in range(8)]
        kept = bank[:KEPT]
        product = bank[KEPT:]
        def self_ps(f):
            return product[1] if isinstance(f, int) and f == 0 else kept[1]

        def aggw_ps(f, u):
            return product[u % 2] if isinstance(f, int) and f < 4 else kept[2 + u % 2]

        staged = [sem(f"staged{i}") for i in range(STAGES)]
        x_loaded = [sem(f"x_loaded{i}") for i in range(2)]
        turned = sem("turned")
        evacuated = sem("evacuated")
        first_reduced = sem("first_reduced")
        first_degree = sem("first_degree")
        first_dinv = sem("first_dinv")
        first_scaled = sem("first_scaled")
        early_multiplied = sem("early_multiplied")
        transposed = sem("transposed")
        summed = sem("summed")
        last_summed = sem("last_summed")
        degree_ready = sem("degree_ready")
        reduced = sem("reduced")
        dinv_ready = sem("dinv_ready")
        scaled = sem("scaled")
        multiplied = sem("multiplied")
        early_added = sem("early_added")
        added = sem("added")
        half_set = sem("half_set")
        const_loaded = sem("const_loaded")
        ident_zero = sem("ident_zero")
        ident_ready = sem("ident_ready")
        xf_loaded = [sem(f"xf_loaded{i}") for i in range(4)]
        agg_done = sem("agg_done")
        squares_loaded = [sem(f"squares_loaded{i}") for i in range(4)]
        xt_ready = sem("xt_ready")
        self_done = sem("self_done")
        self_read = sem("self_read")
        biased = sem("biased")
        aggw_done = sem("aggw_done")
        pre_done = sem("pre_done")
        relu_done = sem("relu_done")
        stats_done = sem("stats_done")
        mv_done = sem("mv_done")
        var_done = sem("var_done")
        rstd_done = sem("rstd_done")
        shift_done = sem("shift_done")
        normed = sem("normed")
        final_normed = sem("final_normed")
        gained = sem("gained")
        last_gained = sem("last_gained")
        finished = sem("finished")
        final_finished = sem("final_finished")
        stored = [sem(f"stored{i}") for i in range(4)]

        def row_chunk(t):
            return (t + FIXED) % H if isinstance(t, int) else t - SPARE

        first_order = [h for pair in zip(range(KEPT, 2 * KEPT), range(KEPT)) for h in pair] + list(range(2 * KEPT, H))

        def row_of(k, t):
            if isinstance(k, int) and k == 1:
                return row_chunk(t) if t < SPARE else first_order[t - SPARE]
            return row_chunk(t)

        def place(h, par):
            return h + SPARE * par if isinstance(h, int) and h >= FIXED else h

        def group_bank(s, c, g):
            return bank[GROUPS * (c % 2) + g] if s == 0 else kept[g]

        block = ctx.enter_context(nc.Block())

        def load_quarter(engine, a, start, u):
            dst = staging[SQ * a:SQ * a + SQ, u, :].rearrange("p (s c) -> p s c", s=SETS)
            return engine.dma_start(dst, moved(adj_view[0, 0, a], start))

        @block.sync
        def _(sp):
            def load(k, h, u, leaves=None, quarters=SYNC_QUARTERS):
                start = h * (ROWS * N) + k * COLS
                if leaves is not None:
                    start = sp.snap(start)
                    sp.lower_val(start * 4)
                    sp.wait_ge(transposed, leaves)
                for a in quarters:
                    load_quarter(sp, a, start, u).then_inc(staged[u], 16)

            def block_loads(k, first=False):
                for u in range(STAGES):
                    if first:
                        sp.wait_ge(turned, (H - STAGES + u + 1) * GROUPS)
                    load(k, row_of(k, u), u, leaves=None if first else (k - 1) * H + (u + 1 - STAGES),
                         quarters=FIRST_QUARTERS if first else SYNC_QUARTERS)
                if first:
                    for t in range(STAGES, H):
                        load(k, row_of(k, t), t % STAGES, leaves=(k - 1) * H + t + (1 - STAGES),
                             quarters=FIRST_QUARTERS)
                    return
                with steps(sp, STAGES, H, STAGES) as t:
                    for u in range(STAGES):
                        load(k, row_chunk(t + u), u, leaves=(k - 1) * H + t + (u + 1 - STAGES))

            for s in range(HALVES):
                for c in range(HALF_CHUNKS):
                    n = s * HALF_CHUNKS + c
                    if n >= STAGES:
                        sp.wait_ge(turned, (n - STAGES + 1) * GROUPS)
                    sp.dma_start(staging[:, n % STAGES, :].rearrange("p (m c) -> p m c", m=TILES),
                                 first_view[0, s, c]).then_inc(staged[n % STAGES], 16)
            block_loads(1, first=True)
            with steps(sp, 2, BLOCKS, 1) as k:
                block_loads(k)

            def x_rows(f, u):
                return sp.dma_start(x_row[u].rearrange("p b d -> p (b d)"), moved(x_view[0], f))

            def x_square_rows(start, u):
                for a in range(QUARTERS):
                    dst = x_squares[u][SQ * a:SQ * a + SQ].rearrange("p (s c) -> p s c", s=SETS)
                    sp.dma_start(dst, moved(x_squares_view[0, a], start)).then_inc(squares_loaded[u], 16)

            def store_rows(f, u):
                rows = sp.snap(f * (ROWS * D))
                sp.lower_val(rows * 4)
                sp.wait_ge(finished, f + 1)
                sp.dma_start(moved(out_view[0], rows), res[u].rearrange("p b d -> p (b d)")).then_inc(stored[u], 16)

            def next_rows(f, u):
                rows = sp.snap((f + 4) * (ROWS * D))
                sp.lower_val(rows * 4)
                sp.wait_ge(relu_done, f + 1)
                x_rows(rows, u).then_inc(xf_loaded[u], 16)
                x_square_rows(rows, u)

            sp.wait_ge(transposed, CHUNKS - H)
            sp.dma_start(x_row[0].rearrange("p (s b) d -> p s (b d)", s=HALVES),
                         first_x_view[0]).then_inc(xf_loaded[0], 16)
            x_square_rows(0, 0)
            for u in range(1, 4):
                x_rows(u * (ROWS * D), u).then_inc(xf_loaded[u], 16)
                x_square_rows(u * (ROWS * D), u)
            next_rows(0, 0)
            next_rows(1, 1)
            next_rows(2, 2)
            sp.wait_ge(finished, 1)
            sp.dma_start(first_out_view[0],
                         res[0].rearrange("p (s b) d -> p s (b d)", s=HALVES)).then_inc(stored[0], 16)
            next_rows(3, 3)
            store_rows(1, 1)
            with steps(sp, 4, H - 4, 4) as f:
                for u in range(4):
                    next_rows(f + u, u)
                    store_rows(f + u - 2, (u - 2) % 4)
            for f in range(H - 6, H - 2):
                store_rows(f, f % 4)
            sp.wait_ge(final_finished, 1)
            sp.dma_start(out_view[H - 2], res[2].rearrange("p b d -> p (b d)")).then_inc(stored[2], 16)
            sp.wait_ge(final_finished, 3)
            sp.dma_start(out_view[H - 1], res[3].rearrange("p b d -> p (b d)")).then_inc(stored[3], 16)
            for u in range(4):
                sp.wait_ge(stored[u], 16 * (H // 4))

        @block.gpsimd
        def _(pool):
            def x_block(k, par, first=False):
                if first and k == 0:
                    pool.dma_start(xs[:, 0].rearrange("p (s b) d -> p s (b d)", s=HALVES),
                                   first_x_view[0]).then_inc(x_loaded[0], 16)
                    return
                if not first:
                    pool.wait_ge(multiplied, (k - 1) * H)
                pool.dma_start(xs[:, par].rearrange("p b d -> p (b d)"),
                               x_view[bass.ds(k, 1)].rearrange("k p c -> (k p) c")).then_inc(x_loaded[par], 16)

            def power(k):
                pool.wait_ge(degree_ready, k + 1)
                nc.gpsimd.tensor_tensor(dinv[:, bass.ds(k, 1), :].rearrange("p k b -> p (k b)"), degree[:, :],
                                        minus_half[:, :], ALU.pow).then_inc(dinv_ready, 1)

            nc.gpsimd.memset(ident, 0.0).then_inc(ident_zero, 1)
            nc.gpsimd.memset(minus_half[:, :], -0.5).then_inc(half_set, 1)
            pool.wait_ge(ident_zero, 1)
            nc.gpsimd.affine_select(out=ident, in_=ident, compare_op=ALU.not_equal, fill=1.0, base=0,
                                    pattern=[[-1, P]], channel_multiplier=1).then_inc(ident_ready, 1)
            x_block(0, 0, first=True)
            pool.wait_ge(half_set, 1)
            for half, degrees_in, dinv_out in ((slice(0, HALF), first_degree, first_dinv),
                                               (slice(HALF, PLANES), degree_ready, dinv_ready)):
                pool.wait_ge(degrees_in, 1)
                nc.gpsimd.tensor_tensor(dinv[:, 0, half], degree[:, half], minus_half[:, half],
                                        ALU.pow).then_inc(dinv_out, 1)
            x_block(1, 1, first=True)
            for dst, src in ((w_sb, weight[:, :]), (ws_sb, self_weight[:, :]),
                             (bias_sb, bias.partition_broadcast(P)), (gamma_sb, gamma.partition_broadcast(P)),
                             (beta_sb, beta.partition_broadcast(P))):
                pool.dma_start(dst, src).then_inc(const_loaded, 16)
            power(1)
            with steps(pool, 2, BLOCKS, 2) as k:
                for par in range(2):
                    x_block(k + par, par)
                    power(k + par)

            pool.wait_ge(const_loaded, 5 * 16)
            bias_b = bias_sb.unsqueeze(1).to_broadcast([P, PLANES, D])
            gamma_b = gamma_sb.unsqueeze(1).to_broadcast([P, PLANES, D])
            beta_b = beta_sb.unsqueeze(1).to_broadcast([P, PLANES, D])

            def gain(f, u):
                pool.wait_ge(normed, f + 1)
                nc.gpsimd.tensor_tensor(res[u], res[u], gamma_b, ALU.mult).then_inc(gained, 1)

            def add_beta(f, u):
                pool.wait_ge(gained, f + 1)
                nc.gpsimd.tensor_tensor(res[u], res[u], beta_b, ALU.add).then_inc(finished, 1)

            def add_bias(f, u):
                pool.wait_ge(self_read, f + 1)
                nc.gpsimd.tensor_tensor(pre[u], pre[u], bias_b, ALU.add).then_inc(biased, 1)

            def output(f, u):
                if not isinstance(f, int) or f < H - 2:
                    add_bias(f + 1, (u + 1) % 4)
                pool.wait_ge(var_done, f + 1)
                nc.gpsimd.tensor_tensor(rstd[u], var_eps[u], minus_half[:, :], ALU.pow).then_inc(rstd_done, 1)
                if isinstance(f, int) and f >= H - 2:
                    if f == H - 1:
                        add_beta(H - 3, 1)
                    else:
                        gain(H - 3, 1)
                elif not (isinstance(f, int) and f == 0):
                    gain(f - 1, (u - 1) % 4)
                    if isinstance(f, int) and f == H - 3:
                        add_bias(H - 1, 3)
                    add_beta(f - 1, (u - 1) % 4)

            add_bias(0, 0)
            for u in range(4):
                output(u, u)
            with steps(pool, 4, H - 4, 4) as f:
                for u in range(4):
                    output(f + u, u)
            for u in range(4):
                output(H - 4 + u, u)

        @block.tensor
        def _(pe):
            def turn_chunk(s, c, u):
                pe.wait_ge(staged[u], (s * (HALF_CHUNKS // STAGES) + c // STAGES + 1) * 16)
                tiles = staging[:, u, :].rearrange("p (m c b) -> p m b c", m=TILES, b=HALF)
                for g in range(GROUPS):
                    if s == 1:
                        pe.wait_ge(evacuated, (HALF_CHUNKS + c - 1) * GROUPS + (g + 1))
                    elif c >= 2:
                        pe.wait_ge(evacuated, (c - 2) * GROUPS + (g + 1))
                    for m in range(ROWS // P):
                        mm = nc.tensor.transpose(group_bank(s, u, g)[:, m * P:m * P + P],
                                                 tiles[:, g // HALF * (ROWS // P) + m, g % HALF, :], ident)
                    mm.then_inc(turned, 1)

            def early(h):
                if h >= KEPT + ROTATING:
                    pe.wait_ge(early_added, h - KEPT - ROTATING + 1)
                for b in range(HALF):
                    mm = nc.tensor.matmul(product[h % ROTATING][:, :], xs[:, 0, b, :],
                                          store[:, b, h * ROWS:(h + 1) * ROWS],
                                          start=b == 0, stop=b == HALF - 1)
                mm.then_inc(early_multiplied, 1)

            def chunk(k, h, u, par, first=False, planes_of=range(PLANES)):
                in_kept = isinstance(h, int) and h < KEPT
                dst = kept[u] if in_kept else product[u]
                rows = bass.ds(place(h, par) * ROWS, ROWS)
                for b in planes_of:
                    if isinstance(h, int) and h == 0 and b < 2 and not first:
                        pe.wait_ge(scaled, 2 * k + (b + 1))
                    mm = nc.tensor.matmul(dst[:, :], xs[:, par, b, :], store[:, b, rows],
                                          start=b == planes_of[0] and (first or not in_kept), stop=b == PLANES - 1,
                                          skip_group_check=in_kept)
                mm.then_inc(multiplied, 1)

            def first_column_block():
                pe.wait_ge(evacuated, H * GROUPS)
                pe.wait_ge(scaled, HALF)
                for h in first_order:
                    if h < KEPT:
                        chunk(0, h, h, 0, first=True)
                        continue
                    if h < KEPT + ROTATING:
                        pe.wait_ge(early_added, EARLY - ROTATING + 1 + (h - KEPT - EARLY) % ROTATING)
                    else:
                        pe.wait_ge(added, h - KEPT - ROTATING + 1)
                    chunk(0, h, h % ROTATING, 0, planes_of=range(HALF if h < KEPT + EARLY else 0, PLANES))

            def column_block(k, par):
                for u in range(KEPT):
                    chunk(k, u, u, par)

                def rotating(h, u):
                    pe.wait_ge(added, k * ADDED + (h - KEPT - ROTATING + 1))
                    chunk(k, h, u, par)

                with steps(pe, KEPT, FIXED, ROTATING) as h:
                    for u in range(ROTATING):
                        rotating(h + u, u)
                for u in range(ROTATING):
                    rotating(FIXED + u, u)

            pe.wait_ge(ident_ready, 1)
            for c in range(HALF_CHUNKS):
                turn_chunk(0, c, c % STAGES)
            for c in range(HALF_CHUNKS):
                turn_chunk(1, c, c % STAGES)
                if c == 0:
                    pe.wait_ge(first_scaled, 1)
                if c < EARLY - EARLY_LEFT:
                    early(KEPT + c)
            for h in range(KEPT + EARLY - EARLY_LEFT, KEPT + EARLY):
                early(h)
            first_column_block()
            with steps(pe, 1, LAST, 2) as k:
                column_block(k, 1)
                column_block(k + 1, 0)

            def plane_rows(ap, f):
                if isinstance(f, int) and f == 0:
                    rows = ap.rearrange("p (s m b) -> p s b m", s=HALVES, b=HALF)
                    return [rows[:, b // HALF, b % HALF, :] for b in range(PLANES)]
                rows = ap.rearrange("p (m b) -> p b m", b=PLANES)
                return [rows[:, b, :] for b in range(PLANES)]

            def self_term(f, u):
                pe.wait_ge(xt_ready, f + 1)
                if isinstance(f, int) and f == 1:
                    pe.wait_ge(agg_done, 2)
                if not (isinstance(f, int) and f <= 1):
                    pe.wait_ge(self_read, f)
                rows = plane_rows(x_t[u % 2], f)
                for b in range(PLANES):
                    mm = nc.tensor.matmul(self_ps(f)[:, b * D:b * D + D], rows[b], ws_sb, start=True, stop=True)
                mm.then_inc(self_done, 1)

            def agg_term(f, u):
                pe.wait_ge(agg_done, f + 1)
                if isinstance(f, int) and f == 1:
                    pe.wait_ge(self_read, 1)
                if not (isinstance(f, int) and f < 2):
                    pe.wait_ge(pre_done, f - 1)
                rows = plane_rows(agg_f[u], f)
                for b in range(PLANES):
                    mm = nc.tensor.matmul(aggw_ps(f, u)[:, b * D:b * D + D], rows[b], w_sb, start=True, stop=True)
                mm.then_inc(aggw_done, 1)

            def output(f, u):
                agg_term(f, u)
                if not isinstance(f, int) or f + 1 < H:
                    self_term(f + 1, (u + 1) % 4)
                h = f + LAG
                if not isinstance(h, int) or h < H:
                    if not isinstance(h, int) or h >= KEPT:
                        pe.wait_ge(agg_done, h - ROTATING + 1)
                        pe.wait_ge(pre_done, f)
                    chunk(LAST, h, h if isinstance(h, int) and h < KEPT else u % ROTATING, 1)

            chunk(LAST, 0, 0, 1)
            pe.wait_ge(const_loaded, 5 * 16)
            pe.wait_ge(added, LAST * ADDED)
            chunk(LAST, 1, 1, 1)
            self_term(0, 0)
            for u in range(4):
                output(u, u)
            with steps(pe, 4, H - 4, 4) as f:
                for u in range(4):
                    output(f + u, u)
            for u in range(4):
                output(H - 4 + u, u)

        @block.scalar
        def _(act):
            def load(k, t):
                kn, tn = (k, t + STAGES) if not isinstance(t, int) or t + STAGES < H else (k + 1, t + STAGES - H)
                start = act.snap(row_of(kn, tn) * (ROWS * N) + kn * COLS)
                act.lower_val(start * 4)
                act.wait_ge(transposed, (k - 1) * H + t + 1)
                for a in SCALAR_QUARTERS:
                    load_quarter(act, a, start, t % STAGES).then_inc(staged[t % STAGES], 16)

            def evacuate(s, c, odd):
                for g in range(GROUPS):
                    act.wait_ge(turned, (s * HALF_CHUNKS + c) * GROUPS + (g + 1))
                    b, h = HALF * s + g % HALF, 2 * c + g // HALF
                    nc.scalar.activation(store[:, b, bass.ds(h * ROWS, ROWS)], group_bank(s, odd, g)[:, :], ACT.Copy,
                                         accum_out=partial[:, b, bass.ds(h, 1)]).then_inc(evacuated, 1)

            def sum_chunk(k, t, par, first=False, count=PLANES):
                act.wait_ge(transposed, (k - 1) * H + t + 1)
                rows = bass.ds(place(row_of(k, t), par) * ROWS, ROWS)
                for b in range(count):
                    if not (first and b < 2):
                        act.wait_ge(summed, (k - 1) * ACT_SUMS + t * PLANES + (b - 1))
                    nc.scalar.activation(junk[:, b % 2, :], store[:, b, rows], ACT.Copy,
                                         accum_out=partial[:, b, bass.ds(t, 1)]).then_inc(summed, 1)

            def sum_block(k, par, first=False, last=False):
                act.wait_ge(degree_ready, k)
                for u in range(STAGES):
                    if not first:
                        load(k, u)
                    sum_chunk(k, u, par, first=first and u == 0)
                if first:
                    for t in range(STAGES, H - STAGES):
                        sum_chunk(k, t, par)
                else:
                    with steps(act, STAGES, H - STAGES, STAGES) as t:
                        for u in range(STAGES):
                            load(k, t + u)
                            sum_chunk(k, t + u, par)
                for t in range(H - STAGES, H):
                    if not last and not first and t < H - 2:
                        load(k, t)
                    sum_chunk(k, t, par, count=PLANES if t < H - 1 else PLANES - DVE_PLANES)
                if first:
                    load(k, H - 4)
                    load(k, H - 3)
                if not last:
                    load(k, H - 2)
                    load(k, H - 1)

            for s in range(HALVES):
                with steps(act, 0, HALF_CHUNKS - STAGES, 2) as c:
                    evacuate(s, c, 0)
                    evacuate(s, c + 1, 1)
                for u in range(STAGES):
                    evacuate(s, HALF_CHUNKS - STAGES + u, u % 2)
            sum_block(1, 1, first=True)
            with steps(act, 2, BLOCKS - 2, 2) as k:
                sum_block(k, 0)
                sum_block(k + 1, 1)
            sum_block(LAST - 1, 0)
            sum_block(LAST, 1, last=True)

            def copy_self(f, u):
                if not (isinstance(f, int) and f < 4):
                    act.wait_ge(normed, f - 3)
                act.wait_ge(self_done, f + 1)
                nc.scalar.activation(pre[u], planes(self_ps(f)[:, :]), ACT.Copy).then_inc(self_read, 1)

            def normalise(f, u):
                act.wait_ge(shift_done, f + 1)
                if not (isinstance(f, int) and f < 4):
                    act.wait_ge(stored[u], 16 * (f // 4))
                for b in range(DVE_PLANES if isinstance(f, int) and f == H - 1 else 0, PLANES):
                    last = nc.scalar.activation(res[u][:, b, :], pre[u][:, b, :], ACT.Identity,
                                                scale=rstd[u][:, b:b + 1], bias=shift[u][:, b:b + 1])
                last.then_inc(normed, 1)

            def output(f, u):
                if isinstance(f, int) and f == H - 2:
                    copy_self(f + 1, (u + 1) % 4)
                if not (isinstance(f, int) and f == 0):
                    normalise(f - 1, (u - 1) % 4)
                if not isinstance(f, int) or f < H - 2:
                    copy_self(f + 1, (u + 1) % 4)

            copy_self(0, 0)
            for u in range(4):
                output(u, u)
            with steps(act, 4, H - 4, 4) as f:
                for u in range(4):
                    output(f + u, u)
            for u in range(4):
                output(H - 4 + u, u)
            normalise(H - 1, 3)

        @block.vector
        def _(dve):
            def transpose(k, t, par):
                u = t % STAGES
                dve.wait_ge(staged[u], ((k - 1) * (H // STAGES) + t // STAGES + 2) * (16 * QUARTERS))
                at = place(row_of(k, t), par) * ROWS
                dst = store[:, :, at:at + ROWS].rearrange("p b (s r) -> p s b r", r=SQ)
                src = staging[:, u, :].rearrange("p (s c b) -> p s b c", s=SETS, b=PLANES)
                nc.vector.transpose(dst, src).then_inc(transposed, 1)

            def sum_last(k, par):
                dve.wait_ge(degree_ready, k)
                dve.wait_ge(transposed, k * H)
                at = place(row_of(k, H - 1), par) * ROWS
                nc.vector.tensor_reduce(partial[:, PLANES - DVE_PLANES:, H - 1],
                                        store[:, PLANES - DVE_PLANES:, at:at + ROWS],
                                        AX_X, ALU.add).then_inc(last_summed, 1)

            def degree_of(k):
                dve.wait_ge(summed, k * ACT_SUMS)
                dve.wait_ge(last_summed, k)
                dve.wait_ge(dinv_ready, k)
                nc.vector.tensor_reduce(degree[:, :], partial[:, :, :], AX_X, ALU.add).then_inc(reduced, 1)
                dve.wait_ge(reduced, k + 1)
                nc.vector.tensor_scalar(degree[:, :], degree[:, :], 1.0, None, ALU.add).then_inc(degree_ready, 1)

            def scale_block(k, par):
                dve.wait_ge(x_loaded[par], (k // 2) * 16 + 16)
                dve.wait_ge(dinv_ready, k + 1)
                d = dinv[:, bass.ds(k, 1), :].rearrange("p k b -> p (k b)").unsqueeze(2)
                for b, n in ((0, 1), (1, PLANES - 1)):
                    nc.vector.tensor_tensor(xs[:, par, b:b + n], xs[:, par, b:b + n],
                                            d[:, b:b + n].to_broadcast([P, n, D]), ALU.mult).then_inc(scaled, 1)

            def add(k, h, u):
                dve.wait_ge(multiplied, k * H + h + 1)
                dve.wait_ge(added, (k - 1) * ADDED + (h - KEPT + 1))
                a = agg[:, bass.ds(h - KEPT, 1), :].rearrange("p h r -> p (h r)")
                nc.vector.tensor_tensor(a, a, product[u][:, :], ALU.add).then_inc(added, 1)

            def refill(k, h, par):
                dve.wait_ge(multiplied, k * H + h + 1)
                t = h + AHEAD - H
                if t < H:
                    transpose(k + 1, t, 1 - par)
                else:
                    transpose(k + 2, t - H, par)

            def column_block(k, par, last=False):
                for h in range(H):
                    if h == FIXED:
                        degree_of(k + 1)
                    if h >= KEPT:
                        add(k, h, (h - KEPT) % ROTATING)
                    if h == FIXED:
                        scale_block(k + 1, 1 - par)
                    if not (last and h >= FIXED):
                        refill(k, h, par)
                    if h == FIXED - 1:
                        sum_last(k + 1, 1 - par)

            def half_degrees(s, sums, reduced_sem, degrees):
                half = slice(HALF * s, HALF * s + HALF)
                dve.wait_ge(evacuated, sums)
                nc.vector.tensor_reduce(degree[:, half], partial[:, half, :], AX_X, ALU.add).then_inc(reduced_sem, 1)
                dve.wait_ge(reduced_sem, 1)
                nc.vector.tensor_scalar(degree[:, half], degree[:, half], 1.0, None, ALU.add).then_inc(degrees, 1)

            def half_scale(s, dinvs, scales):
                half = slice(HALF * s, HALF * s + HALF)
                dve.wait_ge(x_loaded[0], 16)
                dve.wait_ge(dinvs, 1)
                d = dinv[:, 0, half].unsqueeze(2).to_broadcast([P, HALF, D])
                nc.vector.tensor_tensor(xs[:, 0, half], xs[:, 0, half], d, ALU.mult).then_inc(scales, HALF if s else 1)

            def early_copy(h):
                dve.wait_ge(early_multiplied, h - KEPT + 1)
                nc.vector.tensor_copy(agg[:, h - KEPT, :], product[h % ROTATING][:, :]).then_inc(early_added, 1)

            def first_column_block():
                for i, h in enumerate(first_order):
                    if i == FIXED:
                        degree_of(1)
                    dve.wait_ge(multiplied, i + 1)
                    if h >= KEPT + EARLY:
                        nc.vector.tensor_copy(agg[:, h - KEPT, :], product[h % ROTATING][:, :]).then_inc(added, 1)
                    elif h >= KEPT:
                        dve.wait_ge(early_added, h - KEPT + 1)
                        nc.vector.tensor_tensor(agg[:, h - KEPT, :], agg[:, h - KEPT, :], product[h % ROTATING][:, :],
                                                ALU.add).then_inc(added, 1)
                    if i == FIXED:
                        scale_block(1, 1)
                    if i < FIXED:
                        transpose(1, i + SPARE, 1)
                    else:
                        transpose(2, i - FIXED, 0)
                    if i == FIXED - 1:
                        sum_last(1, 1)

            half_degrees(0, HALF_CHUNKS * GROUPS, first_reduced, first_degree)
            half_scale(0, first_dinv, first_scaled)
            for h in range(KEPT, KEPT + EARLY - EARLY_LEFT):
                early_copy(h)
            transpose(1, 0, 1)
            for h in range(KEPT + EARLY - EARLY_LEFT, KEPT + EARLY - 2):
                early_copy(h)
            half_degrees(1, H * GROUPS, reduced, degree_ready)
            early_copy(KEPT + EARLY - 2)
            half_scale(1, dinv_ready, scaled)
            early_copy(KEPT + EARLY - 1)
            transpose(1, 1, 1)
            first_column_block()
            with steps(dve, 1, LAST - 2, 2) as k:
                column_block(k, 1)
                column_block(k + 1, 0)
            column_block(LAST - 2, 1)
            column_block(LAST - 1, 0, last=True)

            gamma_b = gamma_sb.unsqueeze(1).to_broadcast([P, PLANES, D])
            beta_b = beta_sb.unsqueeze(1).to_broadcast([P, PLANES, D])

            def collect(h, u):
                if not (isinstance(h, int) and h < 4):
                    dve.wait_ge(aggw_done, h - 3)
                dve.wait_ge(multiplied, LAST * H + h + 1)
                if isinstance(h, int) and h < KEPT:
                    nc.vector.tensor_copy(agg_f[u], kept[h][:, :]).then_inc(agg_done, 1)
                else:
                    a = agg[:, bass.ds(h - KEPT, 1), :].rearrange("p h r -> p (h r)")
                    nc.vector.tensor_tensor(agg_f[u], a, product[u % ROTATING][:, :], ALU.add).then_inc(agg_done, 1)

            def turn_x(f, u):
                if not (isinstance(f, int) and f < 2):
                    dve.wait_ge(self_done, f - 1)
                dve.wait_ge(squares_loaded[u], (16 * QUARTERS) * (f // 4) + 16 * QUARTERS)
                nc.vector.transpose(x_t[u % 2], x_squares[u]).then_inc(xt_ready, 1)

            def shift_of(f, u):
                dve.wait_ge(rstd_done, f + 1)
                nc.vector.scalar_tensor_tensor(shift[u], mean_var[u][:, :, 0], -1.0, rstd[u],
                                               ALU.mult, ALU.mult).then_inc(shift_done, 1)

            def output(f, u):
                final = isinstance(f, int) and f == H - 1
                dve.wait_ge(biased, f + 1)
                dve.wait_ge(aggw_done, f + 1)
                for b in range(PLANES):
                    scale = dinv[:, bass.ds(f, 1), b:b + 1].rearrange("p k b -> p (k b)")
                    last = nc.vector.scalar_tensor_tensor(pre[u][:, b, :], aggw_ps(f, u)[:, b * D:b * D + D], scale,
                                                          pre[u][:, b, :], ALU.mult, ALU.add)
                last.then_inc(pre_done, 1)
                if not (isinstance(f, int) and f == 0) and not final:
                    shift_of(f - 1, (u - 1) % 4)
                dve.wait_ge(xf_loaded[u], 16 * (f // 4) + 16)
                dve.wait_ge(pre_done, f + 1)
                nc.vector.scalar_tensor_tensor(pre[u].rearrange("p b d -> p (b d)"),
                                               pre[u].rearrange("p b d -> p (b d)"), 0.0,
                                               x_row[u].rearrange("p b d -> p (b d)"),
                                               ALU.max, ALU.add).then_inc(relu_done, 1)
                if final:
                    shift_of(f - 1, (u - 1) % 4)
                dve.wait_ge(relu_done, f + 1)
                for b in range(PLANES):
                    last = nc.vector.bn_stats(stats[u][:, b, :], pre[u][:, b, :])
                last.then_inc(stats_done, 1)
                h = f + LAG
                dve.wait_ge(stats_done, f + 1)
                if not isinstance(h, int) or h < H:
                    turn_x(h, (u + LAG) % 4)
                for b in range(PLANES):
                    last = nc.vector.bn_aggr(mean_var[u][:, b, :], stats[u][:, b, :])
                last.then_inc(mv_done, 1)
                dve.wait_ge(mv_done, f + 1)
                nc.vector.tensor_scalar(var_eps[u], mean_var[u][:, :, 1], EPS, None, ALU.add).then_inc(var_done, 1)
                if not isinstance(h, int) or h < H:
                    collect(h, (u + LAG) % 4)

            for h in range(LAG):
                turn_x(h, h)
            for h in range(LAG):
                collect(h, h)
            dve.wait_ge(const_loaded, 5 * 16)
            for f in range(4):
                output(f, f)
            with steps(dve, 4, H - 4, 4) as f:
                for u in range(4):
                    output(f + u, u)
            for u in range(4):
                output(H - 4 + u, u)
            dve.wait_ge(normed, H - 1)
            nc.vector.tensor_tensor(res[2], res[2], gamma_b, ALU.mult).then_inc(last_gained, 1)
            dve.wait_ge(last_gained, 1)
            nc.vector.tensor_tensor(res[2], res[2], beta_b, ALU.add).then_inc(final_finished, 1)
            shift_of(H - 1, 3)
            dve.wait_ge(shift_done, H)
            dve.wait_ge(stored[3], 16 * (H // 4 - 1))
            for b in range(DVE_PLANES):
                last = nc.vector.tensor_scalar(res[3][:, b, :], pre[3][:, b, :], rstd[3][:, b:b + 1],
                                               shift[3][:, b:b + 1], ALU.mult, ALU.add)
            last.then_inc(final_normed, 1)
            parts = (slice(0, DVE_PLANES), slice(DVE_PLANES, PLANES))
            for part, ready, n in zip(parts, (final_normed, normed), (1, H)):
                dve.wait_ge(ready, n)
                nc.vector.tensor_tensor(res[3][:, part], res[3][:, part], gamma_b[:, part],
                                        ALU.mult).then_inc(last_gained, 1)
            for i, part in enumerate(parts):
                dve.wait_ge(last_gained, i + 2)
                nc.vector.tensor_tensor(res[3][:, part], res[3][:, part], beta_b[:, part],
                                        ALU.add).then_inc(final_finished, 1)


_INS = ["x", "adj", "L0_gnn_weight", "L0_gnn_self_weight", "L0_gnn_bias", "L0_gnn_ln_gamma", "L0_gnn_ln_beta"]
_OUTS = [((8192, 128), "float32")]


def kernel(**inputs):
    import numpy as _np
    import concourse.bacc as _bacc
    from concourse import mybir as _mybir
    from concourse.bass_utils import run_bass_kernel_spmd as _run

    nc = _bacc.Bacc("TRN2", target_bir_lowering=False, num_devices=1)
    arrays, args = {}, []
    for name in _INS:
        a = _np.ascontiguousarray(inputs[name])
        arrays[f"in_{name}_dram"] = a
        args.append(nc.dram_tensor(f"in_{name}_dram", a.shape, _mybir.dt.from_np(a.dtype), kind="ExternalInput").ap())
    for i, (shape, dtype) in enumerate(_OUTS):
        dt = _mybir.dt.from_np(_np.dtype(dtype))
        args.append(nc.dram_tensor(f"out_{i}_dram", shape, dt, kind="ExternalOutput").ap())
    gcn_kernel(nc, *args)
    r = _run(nc, [arrays], core_ids=[0])
    return r.results[0]["out_0_dram"]
```
